# Optimizing a Trainium2 kernel written in Bass

```python
import numpy as np
import jax
import jax.numpy as jnp

def _softmax(x, axis=-1):
    return jax.nn.softmax(x, axis=axis)
def _gelu(x):
    return jax.nn.gelu(x, approximate=True)
def _silu(x):
    return jax.nn.silu(x)
def _sigmoid(x):
    return jax.nn.sigmoid(x)
def _layernorm(x, axis=-1, eps=1e-5):
    m = jnp.mean(x, axis=axis, keepdims=True)
    v = jnp.var(x, axis=axis, keepdims=True)
    return (x - m) / jnp.sqrt(v + eps)
def _scatter_add(tgt, idx, src, axis=0):
    return tgt.at[idx].add(src)
def _segment_sum(src, seg, n):
    return jax.ops.segment_sum(src, seg, n)

kernel_name = 'mk_conv_preact_d1_conv_nchw128_79d41f'

def setup_inputs(seed: int = 0):
    np.random.seed(seed)
    _w = jnp.asarray
    def _rec_inputs():
        import jax
        import jax.numpy as jnp
        _gk = jax.random.key(seed)
        x = -8.268e-05 + 0.9999 * jax.random.normal(jax.random.fold_in(_gk, 1), (8, 128, 224, 224), jnp.float32)
        return x
    x = _rec_inputs()
    def _L0_conv_setup():
        import jax, jax.numpy as jnp
        import numpy as np
        WS = 7
        NUM_HEADS = 4
        key = jax.random.key(seed)
        k1, k2, k3 = jax.random.split(key, 3)
        B, C, H, W = (8, 128, 224, 224)
        x = jax.random.normal(k1, (B, C, H, W), dtype=jnp.float32)
        w_qkv = jax.random.normal(k2, (3 * C, C), dtype=jnp.float32) * C ** (-0.5)
        w_proj = jax.random.normal(k3, (C, C), dtype=jnp.float32) * C ** (-0.5)
        return {'x': x, 'w_qkv': w_qkv, 'w_proj': w_proj}
    _L0_conv_all = _L0_conv_setup()
    _L0_conv_in = {k: v for k, v in _L0_conv_all.items() if k in ('w_qkv', 'w_proj', )}
    del _L0_conv_all

    return {
        "x": x,
        "L0_conv_w_qkv": _L0_conv_in["w_qkv"],
        "L0_conv_w_proj": _L0_conv_in["w_proj"],
    }

def reference(x, L0_conv_w_qkv, L0_conv_w_proj):
    import jax
    import jax.numpy as jnp
    def _L0_conv_ref(x, w_qkv, w_proj):
        import jax, jax.numpy as jnp
        import numpy as np
        WS = 7
        NUM_HEADS = 4
        B, C, H, W = x.shape
        ws = WS
        nh = NUM_HEADS
        hd = C // nh
        scale = hd ** (-0.5)
        H_pad = (ws - H % ws) % ws
        W_pad = (ws - W % ws) % ws
        if H_pad > 0 or W_pad > 0:
            x = jnp.pad(x, ((0, 0), (0, 0), (0, H_pad), (0, W_pad)))
        H2, W2 = (x.shape[2], x.shape[3])
        nWh, nWw = (H2 // ws, W2 // ws)
        xw = x.reshape(B, C, nWh, ws, nWw, ws)
        xw = xw.transpose(0, 2, 4, 1, 3, 5).reshape(B * nWh * nWw, C, ws, ws)
        Bwin = xw.shape[0]
        N = ws * ws
        qkv = jnp.einsum('bcxy,oc->boxy', xw, w_qkv).reshape(Bwin, 3 * C, N)
        qkv = qkv.transpose(0, 2, 1)
        q, k, v = jnp.split(qkv, 3, axis=2)
        q = q.reshape(Bwin, N, nh, hd)
        k = k.reshape(Bwin, N, nh, hd)
        v = v.reshape(Bwin, N, nh, hd)
        scores = jnp.einsum('bnhd,bmhd->bnmh', q, k) * scale
        attn = jax.nn.softmax(scores, axis=-1)
        out = jnp.einsum('bnmh,bmhd->bnhd', attn, v)
        out = out.reshape(Bwin, N, C).transpose(0, 2, 1).reshape(Bwin, C, ws, ws)
        out = out.reshape(B, nWh, nWw, C, ws, ws).transpose(0, 3, 1, 4, 2, 5).reshape(B, C, H2, W2)
        out = jnp.einsum('bchw,oc->bohw', out, w_proj)
        if H_pad > 0 or W_pad > 0:
            out = out[:, :, :H, :W]
        return out

    def _gn(v, G=32, eps=1e-5):
        B_, C_, H_, W_ = v.shape
        g = v.reshape(B_, G, C_ // G, H_, W_)
        m = jnp.mean(g, axis=(2, 3, 4), keepdims=True)
        s = jnp.var(g, axis=(2, 3, 4), keepdims=True)
        return ((g - m) / jnp.sqrt(s + eps)).reshape(v.shape)

    def _ln_c(v, eps=1e-6):
        m = jnp.mean(v, axis=1, keepdims=True)
        s = jnp.var(v, axis=1, keepdims=True)
        return (v - m) / jnp.sqrt(s + eps)

    def _ln_t(v, eps=1e-5):
        m = jnp.mean(v, axis=-1, keepdims=True)
        s = jnp.var(v, axis=-1, keepdims=True)
        return (v - m) / jnp.sqrt(s + eps)

    def _to_tokens(v):
        B_, C_, H_, W_ = v.shape
        return v.reshape(B_, C_, H_ * W_).transpose(0, 2, 1)
    def _from_tokens(t, like):
        B_, C_, H_, W_ = like.shape
        return t.transpose(0, 2, 1).reshape(B_, C_, H_, W_)

    x = x + _L0_conv_ref(_gn(x), L0_conv_w_qkv, L0_conv_w_proj)
    return x


_drawn_inputs = setup_inputs


def setup_inputs(seed=0):
    import zlib

    import numpy as np

    out = dict(_drawn_inputs(seed))
    spreads = {}
    factors = {}
    for name, (base, spread) in spreads.items():
        noise = np.random.default_rng([zlib.crc32(name.encode()), seed]).standard_normal(out[name].shape)
        drawn = base * np.exp(spread * noise) if base else spread * noise
        out[name] = jnp.asarray(drawn.astype(out[name].dtype))
    for name, factor in factors.items():
        out[name] = (out[name] * factor).astype(out[name].dtype)
    return out
```

```python
import concourse.bass as bass
from concourse import mybir
from contextlib import ExitStack


def window_attention_groupnorm_kernel(nc, x, w_qkv_t, w_proj_t, group_mean, out):
    FP32 = mybir.dt.float32
    ALU = mybir.AluOpType
    ACT = mybir.ActivationFunctionType
    AX = mybir.AxisListType

    B, C, H, W = x.shape
    WS = 7
    N = WS * WS
    NH = 4
    HD = C // NH
    SCALE = HD ** -0.5
    EPS = 1e-5
    GP = 64
    P = 128
    assert C == P and H % WS == 0 and W % WS == 0

    STRIPS = H // WS
    STRIP = WS * W
    OCT = 8
    PAIRS = OCT // 2
    OPS = W // WS // OCT
    OW = OCT * WS
    TOK = OCT * N
    COLS = PAIRS * N
    NSTRIP = B * STRIPS
    NOCT = NSTRIP * OPS
    SLOTS = 2
    BODY = SLOTS * OPS
    ITERS = NSTRIP // SLOTS
    BANK = 512
    RING = 4

    SCH = 2 * STRIP
    SN = H * W // SCH
    SBUFS = 4
    BN = 448
    BNS = SCH // BN

    x_strip = x.rearrange("b c (s r) w -> b c s (r w)", r=WS)
    out_strip = out.rearrange("b c (s r) w -> b c s (r w)", r=WS)
    x_chunk = x.rearrange("b c (s r) w -> b c s (r w)", r=2 * WS)

    ctx = ExitStack()
    with ctx:
        def sb(name, shape):
            return ctx.enter_context(nc.sbuf_tensor(name, shape, FP32))

        def pb(name, shape):
            return ctx.enter_context(nc.psum_tensor(name, shape, FP32))

        def sem(name):
            return ctx.enter_context(nc.semaphore(name))

        w_qkv = sb("w_qkv", [P, 3 * C])
        w_proj = sb("w_proj", [P, C])
        gmat = sb("gmat", [P, P])
        x_stat = sb("x_stat", [P, SBUFS, SCH])
        bn = sb("bn", [P, SN * BNS, 6])
        mv = sb("mv", [P, 2])
        mv_all = sb("mv_all", [P, 2, B])
        gmean = sb("gmean", [P, B])
        dev = sb("dev", [P, B])
        dev2 = sb("dev2", [P, B])
        spread = sb("spread", [P, B])
        gvar = sb("gvar", [P, B])
        minus_half = sb("minus_half", [P, B])
        rstd = sb("rstd", [P, B])
        gm_rstd = sb("gm_rstd", [P, B])
        coef_all = sb("coef_all", [P, B, 2])
        coef = sb("coef", [P, SLOTS, 2])

        x_in = sb("x_in", [P, SLOTS, STRIP])
        x_out = sb("x_out", [P, SLOTS, STRIP])
        xn = sb("xn", [P, 2, OCT, GP])
        qk = sb("qk", [P, 2, 2, OCT, GP])
        v_sb = sb("v_sb", [P, RING, PAIRS, C])
        att = sb("att", [P, RING, NH, COLS])
        smax = sb("smax", [P, COLS])
        half = sb("half", [P, 2, COLS])
        den = sb("den", [P, 2, COLS])
        lden = sb("lden", [P, COLS])
        rden = sb("rden", [P, 2, COLS])
        ao = sb("ao", [P, 2, OCT, N])

        ps_all = pb("ps_all", [P, 8, BANK])
        ps_s = ps_all[:, 0:4, 0:COLS]
        VB, KB, QB, OB = 4, 5, 6, 7

        s_w = sem("weights_loaded")
        s_passed = sem("waits_passed")
        s_xs = [sem(f"stat_loaded{i}") for i in range(SBUFS)]
        s_bn = sem("bn_done")
        s_agg = sem("bn_aggregated")
        s_mv = sem("mean_var_kept")
        s_gm = sem("group_mean_ready")
        s_c = sem("coef_steps_dve")
        s_gv = sem("group_var_ready")
        s_cp = sem("coef_steps_pool")
        s_pad = sem("pads_zeroed")
        s_x = [sem(f"strip_loaded{i}") for i in range(SLOTS)]
        s_st = [sem(f"strip_stored{i}") for i in range(SLOTS)]
        s_cc = sem("coef_chosen")
        s_xn = sem("normalised")
        s_qk_ps = sem("qk_in_psum")
        s_v_ps = sem("v_in_psum")
        s_qk = sem("qk_copied")
        s_v = sem("v_copied")
        s_s = sem("scores_ready")
        s_max = sem("max_ready")
        s_sub = sem("max_subtracted")
        s_e = sem("exp_ready")
        s_half = sem("half_sums_ready")
        s_den = sem("denominator_ready")
        s_ln = sem("log_ready")
        s_r = sem("reciprocal_ready")
        s_a = sem("weights_normalised")
        s_o_ps = sem("attended_in_psum")
        s_o = sem("attended_copied")
        s_p = sem("projected")
        s_res = sem("residual_added")

        def need(eng, semaphore, value):
            if not isinstance(value, int) or value > 0:
                eng.wait_ge(semaphore, value)

        def wait_alone(eng, *waits):
            for semaphore, value in waits:
                need(eng, semaphore, value)
            eng.sem_inc(s_passed, 1)

        def iterations(eng, body):
            body(0)
            with eng.Fori(1, ITERS - 1) as i:
                body(i)
            body(ITERS - 1)

        def octet_pixels(buffer, slot, o):
            part = buffer[:, slot, :].rearrange("p (r w c) -> p w r c", r=WS, c=WS)
            return part[:, o * OCT:(o + 1) * OCT, :, :]

        block = ctx.enter_context(nc.Block())

        @block.sync
        def _(sp):
            sp.dma_start(w_qkv[:, :], w_qkv_t).then_inc(s_w, 16)
            sp.dma_start(w_proj[:, :], w_proj_t).then_inc(s_w, 16)
            sp.dma_start(gmat[:, :], group_mean).then_inc(s_w, 16)

            def stat_load(b, n):
                sp.dma_start(x_stat[:, n % SBUFS, :], x_chunk[b, :, n, :]
                             if isinstance(b, int) else
                             x_chunk[bass.ds(b, 1), :, n, :].rearrange("a c w -> (a c) w")
                             ).then_inc(s_xs[n % SBUFS], 16)

            for n in range(SN):
                if n >= SBUFS:
                    sp.wait_ge(s_bn, n - SBUFS + 1)
                stat_load(0, n)
            with sp.Fori(1, B) as b:
                for n in range(SN):
                    sp.wait_ge(s_bn, b * SN + (n - SBUFS + 1))
                    stat_load(b, n)

            def at(view, s):
                if isinstance(s, int):
                    return view[s // STRIPS, :, s % STRIPS, :]
                return view[bass.ds(s // STRIPS, 1), :, bass.ds(s % STRIPS, 1), :].rearrange(
                    "a c s w -> (a c s) w")

            def load(s, slot):
                sp.dma_start(x_in[:, slot, :], at(x_strip, s)).then_inc(s_x[slot], 16)

            def body(i):
                for slot in range(SLOTS):
                    s = i * SLOTS + slot
                    sp.wait_ge(s_res, s * OPS + OPS)
                    sp.dma_start(at(out_strip, s), x_out[:, slot, :]).then_inc(s_st[slot], 16)
                    if not (isinstance(i, int) and i == ITERS - 1):
                        load(s + SLOTS, slot)

            for slot in range(SLOTS):
                load(slot, slot)
            iterations(sp, body)
            for slot in range(SLOTS):
                sp.wait_ge(s_st[slot], 16 * ITERS)

        @block.gpsimd
        def _(pool):
            pool.memset(xn[:, :, :, :], 0.0).then_inc(s_pad, 1)
            pool.memset(qk[:, :, :, :, :], 0.0).then_inc(s_pad, 1)
            pool.memset(minus_half[:, :], -0.5).then_inc(s_pad, 1)
            pool.wait_ge(s_pad, 3)
            pool.wait_ge(s_c, 5)
            pool.tensor_tensor(rstd[:, :], gvar[:, :], minus_half[:, :], ALU.pow).then_inc(s_cp, 1)
            pool.wait_ge(s_cp, 1)
            pool.tensor_tensor(gm_rstd[:, :], gmean[:, :], rstd[:, :], ALU.mult).then_inc(s_cp, 1)
            pool.tensor_copy(coef_all[:, :, 0], rstd[:, :]).then_inc(s_cp, 1)
            pool.wait_ge(s_cp, 3)
            pool.tensor_scalar(coef_all[:, :, 1], gm_rstd[:, :], -1.0, 0.0, ALU.mult,
                               ALU.add).then_inc(s_cp, 1)
            pool.wait_ge(s_cp, 4)

            def choose_coef(i, slot):
                s = i * SLOTS + slot
                b = s // STRIPS
                src = coef_all[:, b, :] if isinstance(b, int) else \
                    coef_all[:, bass.ds(b, 1), :].rearrange("p a t -> p (a t)")
                pool.tensor_copy(coef[:, slot, :], src).then_inc(s_cc, 1)
                pool.wait_ge(s_cc, s + 1)

            def normalise(i, o, slot_iter):
                slot = o // OPS
                if o % OPS == 0:
                    choose_coef(i, slot)
                    pool.wait_ge(s_x[slot], 16 * i + 16)
                g = i * BODY + o
                wait_alone(pool, (s_v_ps, g - 1))
                dst = xn[:, o % 2, :, 0:N].rearrange("p w (r c) -> p w r c", r=WS)
                pool.tensor_scalar(dst, octet_pixels(x_in, slot, o % OPS), coef[:, slot, 0:1],
                                   coef[:, slot, 1:2], ALU.mult, ALU.add).then_inc(s_xn, 1)

            def sum_heads(i, o):
                g = i * BODY + o
                a = att[:, o % RING, :, :]
                pool.wait_ge(s_e, g + 1)
                pool.tensor_tensor(half[:, :, :], a[:, 0:2, :], a[:, 2:4, :],
                                   ALU.add).then_inc(s_half, 1)
                pool.wait_ge(s_half, g + 1)
                pool.tensor_tensor(den[:, o % 2, :], half[:, 0, :], half[:, 1, :],
                                   ALU.add).then_inc(s_den, 1)

            def body(i):
                for o in range(BODY):
                    if not (isinstance(i, int) and i == ITERS - 1 and o >= BODY - 2):
                        if o + 2 < BODY:
                            normalise(i, o + 2, i)
                        else:
                            normalise(i + 1, o + 2 - BODY, i)
                    sum_heads(i, o)

            normalise(0, 0, 0)
            normalise(0, 1, 0)
            iterations(pool, body)

        @block.scalar
        def _(act):
            def copy_qkv(i, o):
                g = i * BODY + o
                act.wait_ge(s_qk_ps, g + 1)
                src = ps_all[:, KB:QB + 1, 0:TOK].rearrange("p b (w n) -> p b w n", n=N)
                act.activation(qk[:, o % 2, :, :, 0:N], src, ACT.Copy).then_inc(s_qk, 1)
                act.wait_ge(s_v_ps, g + 1)
                act.activation(v_sb[:, o % RING, :, :],
                               ps_all[:, VB, :].rearrange("p (a c) -> p a c", a=PAIRS),
                               ACT.Copy).then_inc(s_v, 1)

            def exp(i, o):
                g = i * BODY + o
                a = att[:, o % RING, :, :]
                act.wait_ge(s_sub, g + 1)
                act.activation(a, a, ACT.Exp, scale=SCALE).then_inc(s_e, 1)

            def reciprocal(i, o):
                g = i * BODY + o
                act.wait_ge(s_den, g + 1)
                act.activation(lden[:, :], den[:, o % 2, :], ACT.Ln).then_inc(s_ln, 1)
                act.wait_ge(s_ln, g + 1)
                act.activation(rden[:, o % 2, :], lden[:, :], ACT.Exp, scale=-1.0).then_inc(s_r, 1)

            def copy_attended(i, o):
                g = i * BODY + o
                act.wait_ge(s_o_ps, g + 1)
                src = ps_all[:, QB:OB + 1, 0:COLS].rearrange("p j (a n) -> p j a n", n=N)
                dst = ao[:, o % 2, :, :].rearrange("p (a j) n -> p j a n", j=2)
                act.activation(dst, src, ACT.Copy).then_inc(s_o, 1)

            def step(i, o, first=False, last=False):
                if not last:
                    copy_qkv(*((i, o + 1) if o + 1 < BODY else (i + 1, 0)))
                before = (i, o - 1) if o else (i - 1, BODY - 1)
                if not first:
                    reciprocal(*before)
                exp(i, o)
                if not first:
                    copy_attended(*before)

            def body(i):
                whole = isinstance(i, int)
                for o in range(BODY):
                    step(i, o, whole and i == 0 and o == 0, whole and i == ITERS - 1 and o == BODY - 1)

            act.wait_ge(s_pad, 3)
            copy_qkv(0, 0)
            iterations(act, body)
            reciprocal(ITERS - 1, BODY - 1)
            copy_attended(ITERS - 1, BODY - 1)

        @block.tensor
        def _(pe):
            pe.wait_ge(s_w, 48)
            pe.wait_ge(s_mv, B)
            pe.matmul(ps_all[:, 0, 0:B], gmat[:, :], mv_all[:, 0, :], start=True,
                      stop=True).then_inc(s_gm, 1)
            pe.wait_ge(s_c, 4)
            pe.matmul(ps_all[:, 1, 0:B], gmat[:, :], spread[:, :], start=True,
                      stop=True).then_inc(s_gv, 1)
            pe.wait_ge(s_c, 5)

            def project_qkv(i, o):
                g = i * BODY + o
                tokens = xn[:, o % 2, :, 0:N]
                pe.wait_ge(s_xn, g + 1)
                need(pe, s_o, g - 2)
                pe.matmul(ps_all[:, QB, 0:TOK], w_qkv[:, 0:C], tokens, start=True, stop=True)
                need(pe, s_res, g - 3)
                pe.matmul(ps_all[:, KB, 0:TOK], w_qkv[:, C:2 * C], tokens, start=True,
                          stop=True).then_inc(s_qk_ps, 1)
                need(pe, s_v, g)
                for a in range(PAIRS):
                    pair = xn[:, o % 2, 2 * a:2 * a + 2, :].rearrange("p j n -> p (j n)")
                    mm = pe.matmul(ps_all[:, VB, a * C:(a + 1) * C], pair, w_qkv[:, 2 * C:3 * C],
                                   start=True, stop=True)
                mm.then_inc(s_v_ps, 1)

            def scores(i, o):
                g = i * BODY + o
                pe.wait_ge(s_qk, g + 1)
                need(pe, s_sub, g)
                for a in range(PAIRS):
                    for j in range(2):
                        for h in range(NH):
                            rows = slice(h * HD, (h + 1) * HD)
                            mm = pe.matmul(ps_s[j * GP:(j + 1) * GP, h, a * N:(a + 1) * N],
                                           qk[rows, o % 2, 0, 2 * a + j, :],
                                           qk[rows, o % 2, 1, 2 * a + j, 0:N],
                                           start=True, stop=True)
                mm.then_inc(s_s, 1)

            def attend(i, o):
                g = i * BODY + o
                wait_alone(pe, (s_a, g + 1), (s_qk, NOCT if isinstance(g, int) and g == NOCT - 1 else g + 2),
                           (s_o, g))
                for a in range(PAIRS):
                    for h in range(NH):
                        for j in range(2):
                            rows = slice(j * GP, j * GP + N)
                            mm = pe.matmul(ps_all[h * HD:(h + 1) * HD, OB if j else QB,
                                                  a * N:(a + 1) * N],
                                           v_sb[rows, o % RING, a, h * HD:(h + 1) * HD],
                                           att[rows, o % RING, h, a * N:(a + 1) * N],
                                           start=True, stop=True)
                mm.then_inc(s_o_ps, 1)

            def project(i, o):
                g = i * BODY + o
                pe.wait_ge(s_o, g + 1)
                need(pe, s_res, g)
                pe.matmul(ps_all[:, KB, 0:TOK], w_proj[:, :], ao[:, o % 2, :, :], start=True,
                          stop=True).then_inc(s_p, 1)

            def step(i, o, g=None):
                scores(i, o)
                if g != NOCT - 1:
                    project_qkv(*((i, o + 1) if o + 1 < BODY else (i + 1, 0)))
                before = (i, o - 1) if o else (i - 1, BODY - 1)
                before2 = (i, o - 2) if o >= 2 else (i - 1, BODY + o - 2)
                if g is None or g >= 2:
                    if g == NOCT - 1:
                        pass
                    pe.wait_ge(s_qk, i * BODY + o + (1 if g == NOCT - 1 else 2))
                    project(*before2)
                if g is None or g >= 1:
                    attend(*before)

            def body(i):
                for o in range(BODY):
                    step(i, o, i * BODY + o if isinstance(i, int) else None)

            pe.wait_ge(s_pad, 3)
            project_qkv(0, 0)
            iterations(pe, body)
            project(ITERS - 1, BODY - 2)
            attend(ITERS - 1, BODY - 1)
            project(ITERS - 1, BODY - 1)

        @block.vector
        def _(dve):
            def statistics(b):
                for n in range(SN):
                    dve.wait_ge(s_xs[n % SBUFS], 16 * (b * (SN // SBUFS) + n // SBUFS + 1))
                    for m in range(BNS):
                        ins = dve.bn_stats(bn[:, n * BNS + m, :],
                                           x_stat[:, n % SBUFS, m * BN:(m + 1) * BN])
                    ins.then_inc(s_bn, 1)
                wait_alone(dve, (s_bn, b * SN + SN))
                dve.bn_aggr(mv[:, :], bn[:, :, :].rearrange("p a b -> p (a b)")).then_inc(s_agg, 1)
                dve.wait_ge(s_agg, b + 1)
                dst = mv_all[:, :, b:b + 1] if isinstance(b, int) else mv_all[:, :, bass.ds(b, 1)]
                dve.tensor_copy(dst, mv[:, :].rearrange("p (t a) -> p t a", a=1)).then_inc(s_mv, 1)

            statistics(0)
            with dve.Fori(1, B) as b:
                statistics(b)
            dve.wait_ge(s_gm, 1)
            dve.tensor_copy(gmean[:, :], ps_all[:, 0, 0:B]).then_inc(s_c, 1)
            dve.wait_ge(s_c, 1)
            dve.wait_ge(s_mv, B)
            dve.tensor_tensor(dev[:, :], mv_all[:, 0, :], gmean[:, :], ALU.subtract).then_inc(s_c, 1)
            dve.wait_ge(s_c, 2)
            dve.tensor_tensor(dev2[:, :], dev[:, :], dev[:, :], ALU.mult).then_inc(s_c, 1)
            dve.wait_ge(s_c, 3)
            dve.tensor_tensor(spread[:, :], mv_all[:, 1, :], dev2[:, :], ALU.add).then_inc(s_c, 1)
            dve.wait_ge(s_gv, 1)
            dve.tensor_scalar(gvar[:, :], ps_all[:, 1, 0:B], EPS, None, ALU.add).then_inc(s_c, 1)

            def subtract_max(i, o):
                g = i * BODY + o
                dve.wait_ge(s_s, g + 1)
                dve.tensor_reduce(smax[:, :], ps_s.rearrange("p h n -> p n h"), AX.X,
                                  ALU.max).then_inc(s_max, 1)
                dve.wait_ge(s_max, g + 1)
                dve.tensor_tensor(att[:, o % RING, :, :], ps_s,
                                  smax[:, :].unsqueeze(1).broadcast_to([P, NH, COLS]),
                                  ALU.subtract).then_inc(s_sub, 1)

            def normalise_weights(i, o):
                g = i * BODY + o
                a = att[:, o % RING, :, :]
                dve.wait_ge(s_r, g + 1)
                dve.tensor_tensor(a, a, rden[:, o % 2, :].unsqueeze(1).broadcast_to([P, NH, COLS]),
                                  ALU.mult).then_inc(s_a, 1)

            def add_residual(i, o):
                g = i * BODY + o
                slot = o // OPS
                if o % OPS == 0:
                    need(dve, s_st[slot], 16 * i)
                dve.wait_ge(s_p, g + 1)
                src = ps_all[:, KB, 0:TOK].rearrange("p (w r c) -> p w r c", w=OCT, c=WS)
                dve.tensor_tensor(octet_pixels(x_out, slot, o % OPS), src,
                                  octet_pixels(x_in, slot, o % OPS), ALU.add).then_inc(s_res, 1)

            def step(i, o, g=None):
                subtract_max(i, o)
                if g is None or g >= 1:
                    normalise_weights(*((i, o - 1) if o else (i - 1, BODY - 1)))
                if g is None or g >= 2:
                    add_residual(*((i, o - 2) if o >= 2 else (i - 1, BODY + o - 2)))

            def body(i):
                for o in range(BODY):
                    step(i, o, i * BODY + o if isinstance(i, int) else None)

            iterations(dve, body)
            normalise_weights(ITERS - 1, BODY - 1)
            add_residual(ITERS - 1, BODY - 2)
            add_residual(ITERS - 1, BODY - 1)


def kernel(x, L0_conv_w_qkv, L0_conv_w_proj):
    import numpy as np
    import concourse.bacc as bacc
    from concourse.bass_utils import run_bass_kernel_spmd

    nc = bacc.Bacc("TRN2", target_bir_lowering=False, num_devices=1)
    arrays = {
        "x": np.ascontiguousarray(x),
        "w_qkv_t": np.ascontiguousarray(np.asarray(L0_conv_w_qkv).T),
        "w_proj_t": np.ascontiguousarray(np.asarray(L0_conv_w_proj).T),
        "group_mean": np.kron(np.eye(32, dtype=np.float32), np.full((4, 4), 0.25, np.float32)),
    }
    dt = mybir.dt.float32
    args = [nc.dram_tensor(n, a.shape, dt, kind="ExternalInput").ap() for n, a in arrays.items()]
    out = nc.dram_tensor("out", arrays["x"].shape, dt, kind="ExternalOutput").ap()
    window_attention_groupnorm_kernel(nc, *args, out)
    r = run_bass_kernel_spmd(nc, [arrays], core_ids=[0])
    return r.results[0]["out"]
```

```python
import concourse.bass as bass
from concourse import mybir
from contextlib import ExitStack


def window_attention_groupnorm_kernel(nc, x, w_qkv_t, w_proj_t, group_mean, out):
    FP32 = mybir.dt.float32
    ALU = mybir.AluOpType
    ACT = mybir.ActivationFunctionType
    AX = mybir.AxisListType

    B, C, H, W = x.shape
    WS = 7
    N = WS * WS
    NH = 4
    HD = C // NH
    SCALE = HD ** -0.5
    EPS = 1e-5
    GP = 64
    P = 128
    assert C == P and H % WS == 0 and W % WS == 0

    STRIPS = H // WS
    STRIP = WS * W
    OCT = 8
    PAIRS = OCT // 2
    OPS = W // WS // OCT
    TOK = OCT * N
    SLOTS = 2
    BODY = SLOTS * OPS
    IPI = STRIPS // SLOTS
    NOCT = B * STRIPS * OPS
    BANK = 512
    PAIR_COLS = BANK // 2
    VRING = 4

    SBUFS = 2
    BN = 448
    SCH = BODY * BN
    SN = H * W // SCH
    LAST_STATS = IPI - 1
    assert SN * SCH == H * W and SN < LAST_STATS + 1 and SN % SBUFS == 0

    x_strip = x.rearrange("b c (s r) w -> b c s (r w)", r=WS)
    out_strip = out.rearrange("b c (s r) w -> b c s (r w)", r=WS)
    x_chunk = x.rearrange("b c h w -> b c (h w)").rearrange("b c (n k) -> b c n k", k=SCH)

    ctx = ExitStack()
    with ctx:
        def sb(name, shape):
            return ctx.enter_context(nc.sbuf_tensor(name, shape, FP32))

        def pb(name, shape):
            return ctx.enter_context(nc.psum_tensor(name, shape, FP32))

        def sem(name):
            return ctx.enter_context(nc.semaphore(name))

        w_qkv = sb("w_qkv", [P, 3 * C])
        w_proj = sb("w_proj", [P, C])
        group = sb("group", [P, P])
        x_stat = sb("x_stat", [P, SBUFS, SCH])
        bn = sb("bn", [P, SN * BODY, 6])
        mv = sb("mv", [P, 2])
        gmean = sb("gmean", [P, 1])
        dev = sb("dev", [P, 1])
        dev2 = sb("dev2", [P, 1])
        spread = sb("spread", [P, 1])
        gvar = sb("gvar", [P, 1])
        minus_half = sb("minus_half", [P, 1])
        gm_rstd = sb("gm_rstd", [P, 1])
        coef_next = sb("coef_next", [P, 2])
        coef = sb("coef", [P, 2])

        x_in = sb("x_in", [P, SLOTS, STRIP])
        x_out = sb("x_out", [P, SLOTS, STRIP])
        xn = sb("xn", [P, 2, OCT, GP])
        keys = sb("keys", [P, 2, OCT, GP])
        queries = sb("queries", [P, 2, OCT, NH, N])
        values = sb("values", [P, VRING, PAIRS, C])
        att = sb("att", [P, 2, PAIRS, NH, N])
        smax = sb("smax", [P, PAIRS, N])
        half = sb("half", [P, PAIRS, 2, N])
        den = sb("den", [P, 2, PAIRS, N])
        rden = sb("rden", [P, PAIRS, N])
        attended = sb("attended", [P, 2, OCT, N])

        ps_s = pb("ps_scores", [P, PAIRS, PAIR_COLS])
        ps_v = pb("ps_v", [P, PAIRS, C])
        ps_k = pb("ps_k", [P, BANK])
        ps_q = pb("ps_q", [P, BANK])
        ps_o = pb("ps_attended", [P, 2, BANK])
        ps_p = pb("ps_projected", [P, BANK])
        GCOL = BANK - 1
        scores_ps = ps_s[:, :, 0:NH * N].rearrange("p a (h n) -> p a h n", h=NH)

        s_w = sem("weights_loaded")
        s_passed = sem("waits_passed")
        s_pad = sem("pads_zeroed")
        s_xs = [sem(f"stat_chunk_loaded{i}") for i in range(SBUFS)]
        s_bn = sem("bn_done")
        s_mv = sem("channel_stats_ready")
        s_gm = sem("group_mean_in_psum")
        s_c = sem("group_steps_done")
        s_gv = sem("group_var_in_psum")
        s_cp = sem("coef_steps_done")
        s_x = [sem(f"strip_loaded{i}") for i in range(SLOTS)]
        s_st = [sem(f"strip_stored{i}") for i in range(SLOTS)]
        s_xn = sem("normalised")
        s_q_ps = sem("q_in_psum")
        s_k_ps = sem("k_in_psum")
        s_v_ps = sem("v_in_psum")
        s_qk = sem("qk_copied")
        s_v = sem("v_copied")
        s_s = sem("scores_ready")
        s_max = sem("max_ready")
        s_sub = sem("max_subtracted")
        s_e = sem("exp_ready")
        s_half = sem("half_sums_ready")
        s_den = sem("denominator_ready")
        s_r = sem("reciprocal_ready")
        s_a = sem("weights_normalised")
        s_o_ps = sem("attended_in_psum")
        s_o = sem("attended_copied")
        s_p = sem("projected")
        s_res = sem("residual_added")

        GROUP_STEPS = 5
        COEF_STEPS = 4

        def need(eng, semaphore, value):
            if not isinstance(value, int) or value > 0:
                eng.wait_ge(semaphore, value)

        def wait_alone(eng, *waits):
            for semaphore, value in waits:
                need(eng, semaphore, value)
            eng.sem_inc(s_passed, 1)

        def octet_pixels(buffer, slot, o):
            part = buffer[:, slot, :].rearrange("p (r w c) -> p w r c", r=WS, c=WS)
            return part[:, o * OCT:(o + 1) * OCT, :, :]

        def ahead(i, o, by):
            return i + (o + by) // BODY, (o + by) % BODY

        def number(i, o):
            return i * BODY + o

        block = ctx.enter_context(nc.Block())

        @block.sync
        def _(sp):
            def one(view, b, s):
                if isinstance(b, int) and isinstance(s, int):
                    return view[b, :, s, :]
                pick = lambda v: slice(v, v + 1) if isinstance(v, int) else bass.ds(v, 1)
                return view[pick(b), :, pick(s), :].rearrange("a c s w -> (a c s) w")

            def load(b, s, slot):
                sp.dma_start(x_in[:, slot, :], one(x_strip, b, s)).then_inc(s_x[slot], 16)

            def stat_load(b, n, buf):
                need(sp, s_bn, (b * SN + n - SBUFS + 1))
                sp.dma_start(x_stat[:, buf, :], one(x_chunk, b, n)).then_inc(s_xs[buf], 16)

            def iteration(b, j, next_strips):
                for slot in range(SLOTS):
                    sp.wait_ge(s_res, number(b * IPI + j, (slot + 1) * OPS))
                    sp.dma_start(one(out_strip, b, j * SLOTS + slot),
                                 x_out[:, slot, :]).then_inc(s_st[slot], 16)
                    if next_strips:
                        load(next_strips[0], next_strips[1] + slot, slot)

            def image(b, behind_next=True, last=False):
                with sp.Fori(0, SN // SBUFS - 1) as turn:
                    for k in range(SBUFS):
                        j = turn * SBUFS + k
                        iteration(b, j, (b, j * SLOTS + SLOTS))
                        if not last:
                            stat_load(b + 1, j + SBUFS, k)
                for j in range(SN - SBUFS, IPI - 1):
                    iteration(b, j, (b, j * SLOTS + SLOTS))
                if behind_next:
                    for n in range(SBUFS):
                        stat_load(b + 2, n, n)
                if not last:
                    iteration(b, IPI - 1, (b + 1, 0))
                else:
                    iteration(b, IPI - 1, None)

            sp.dma_start(w_qkv[:, :], w_qkv_t).then_inc(s_w, 16)
            sp.dma_start(w_proj[:, :], w_proj_t).then_inc(s_w, 16)
            sp.dma_start(group[:, :], group_mean).then_inc(s_w, 16)
            for n in range(SN):
                stat_load(0, n, n % SBUFS)
            for slot in range(SLOTS):
                load(0, slot, slot)
            for n in range(SBUFS):
                stat_load(1, n, n)
            image(0)
            with sp.Fori(1, B - 2) as b:
                image(b)
            image(B - 2, behind_next=False)
            image(B - 1, behind_next=False, last=True)
            for slot in range(SLOTS):
                sp.wait_ge(s_st[slot], 16 * B * IPI)

        @block.gpsimd
        def _(pool):
            pool.memset(xn[:, :, :, :], 0.0).then_inc(s_pad, 1)
            pool.memset(keys[:, :, :, :], 0.0).then_inc(s_pad, 1)
            pool.memset(queries[:, :, :, :, :], 0.0).then_inc(s_pad, 1)
            pool.memset(minus_half[:, :], -0.5).then_inc(s_pad, 1)
            pool.wait_ge(s_pad, 4)

            def coefficients(b):
                done = b * (COEF_STEPS + 1)
                pool.wait_ge(s_c, b * GROUP_STEPS + GROUP_STEPS)
                pool.tensor_tensor(coef_next[:, 0:1], gvar[:, :], minus_half[:, :],
                                   ALU.pow).then_inc(s_cp, 1)
                pool.wait_ge(s_cp, done + 1)
                pool.tensor_tensor(gm_rstd[:, :], gmean[:, :], coef_next[:, 0:1],
                                   ALU.mult).then_inc(s_cp, 1)
                wait_alone(pool, (s_cp, done + 2))
                pool.tensor_scalar(coef_next[:, 1:2], gm_rstd[:, :], -1.0, 0.0, ALU.mult,
                                   ALU.add).then_inc(s_cp, 2)

            def choose(b):
                wait_alone(pool, (s_cp, b * (COEF_STEPS + 1) + COEF_STEPS))
                pool.tensor_copy(coef[:, :], coef_next[:, :]).then_inc(s_cp, 1)
                wait_alone(pool, (s_cp, b * (COEF_STEPS + 1) + COEF_STEPS + 1))

            def normalise(i, o):
                g = number(i, o)
                wait_alone(pool, (s_x[o // OPS], 16 * i + 16), (s_v_ps, g - 1))
                dst = xn[:, o % 2, :, 0:N].rearrange("p w (r c) -> p w r c", r=WS)
                pool.tensor_scalar(dst, octet_pixels(x_in, o // OPS, o % OPS), coef[:, 0:1],
                                   coef[:, 1:2], ALU.mult, ALU.add).then_inc(s_xn, 1)

            def sum_heads(i, o):
                g = number(i, o)
                a = att[:, o % 2, :, :, :]
                pool.wait_ge(s_e, g + 1)
                pool.tensor_tensor(half[:, :, :, :], a[:, :, 0:2, :], a[:, :, 2:4, :],
                                   ALU.add).then_inc(s_half, 1)
                pool.wait_ge(s_half, g + 1)
                pool.tensor_tensor(den[:, o % 2, :, :], half[:, :, 0, :], half[:, :, 1, :],
                                   ALU.add).then_inc(s_den, 1)

            def iteration(i, next_image=None, last=False):
                for o in range(BODY):
                    ni, no = ahead(i, o, 2)
                    if no == 0 and next_image is not None:
                        choose(next_image)
                    if not (last and o + 2 >= BODY):
                        normalise(ni, no)
                    sum_heads(i, o)

            coefficients(0)
            choose(0)
            normalise(0, 0)
            normalise(0, 1)

            def image(b, last=False):
                with pool.Fori(0, LAST_STATS) as j:
                    iteration(b * IPI + j)
                if last:
                    iteration(b * IPI + IPI - 1, last=True)
                else:
                    coefficients(b + 1)
                    iteration(b * IPI + IPI - 1, next_image=b + 1)

            with pool.Fori(0, B - 1) as b:
                image(b)
            image(B - 1, last=True)

        @block.scalar
        def _(act):
            def copy_qk(i, o):
                g = number(i, o)
                act.wait_ge(s_q_ps, g + 1)
                for h in range(NH):
                    rows = slice(h * HD, (h + 1) * HD)
                    act.activation(queries[rows, o % 2, :, h, :],
                                   ps_q[rows, 0:TOK].rearrange("p (w n) -> p w n", n=N), ACT.Copy)
                act.wait_ge(s_k_ps, g + 1)
                act.activation(keys[:, o % 2, :, 0:N],
                               ps_k[:, 0:TOK].rearrange("p (w n) -> p w n", n=N),
                               ACT.Copy).then_inc(s_qk, 1)

            def copy_v(i, o):
                act.wait_ge(s_v_ps, number(i, o) + 1)
                act.activation(values[:, o % VRING, :, :], ps_v[:, :, :], ACT.Copy).then_inc(s_v, 1)

            def exp(i, o):
                a = att[:, o % 2, :, :, :]
                act.wait_ge(s_sub, number(i, o) + 1)
                act.activation(a, a, ACT.Exp, scale=SCALE).then_inc(s_e, 1)

            def copy_attended(i, o):
                act.wait_ge(s_o_ps, number(i, o) + 1)
                src = ps_o[:, :, 0:PAIRS * N].rearrange("p j (a n) -> p j a n", n=N)
                dst = attended[:, o % 2, :, :].rearrange("p (a j) n -> p j a n", j=2)
                act.activation(dst, src, ACT.Copy).then_inc(s_o, 1)

            def iteration(i, first=False, last=False):
                for o in range(BODY):
                    following = not (last and o == BODY - 1)
                    if following:
                        copy_qk(*ahead(i, o, 1))
                    exp(i, o)
                    if following:
                        copy_v(*ahead(i, o, 1))
                    if not (first and o == 0):
                        copy_attended(*ahead(i, o, -1))

            act.wait_ge(s_pad, 4)
            copy_qk(0, 0)
            copy_v(0, 0)
            iteration(0, first=True)
            with act.Fori(1, B * IPI - 1) as i:
                iteration(i)
            iteration(B * IPI - 1, last=True)
            copy_attended(B * IPI - 1, BODY - 1)

        @block.tensor
        def _(pe):
            def group_means(b, projected):
                wait_alone(pe, (s_mv, b + 1), (s_res, projected))
                pe.matmul(ps_p[:, GCOL:GCOL + 1], group[:, :], mv[:, 0:1], start=True,
                          stop=True).then_inc(s_gm, 1)
                pe.wait_ge(s_c, b * GROUP_STEPS + GROUP_STEPS - 1)
                pe.matmul(ps_p[:, GCOL:GCOL + 1], group[:, :], spread[:, :], start=True,
                          stop=True).then_inc(s_gv, 1)
                wait_alone(pe, (s_c, b * GROUP_STEPS + GROUP_STEPS))

            def project_qkv(i, o):
                g = number(i, o)
                tokens = xn[:, o % 2, :, 0:N]
                pe.wait_ge(s_xn, g + 1)
                need(pe, s_qk, g)
                pe.matmul(ps_q[:, 0:TOK], w_qkv[:, 0:C], tokens, start=True,
                          stop=True).then_inc(s_q_ps, 1)
                pe.matmul(ps_k[:, 0:TOK], w_qkv[:, C:2 * C], tokens, start=True,
                          stop=True).then_inc(s_k_ps, 1)
                need(pe, s_v, g)
                for a in range(PAIRS):
                    pair = xn[:, o % 2, 2 * a:2 * a + 2, :].rearrange("p j n -> p (j n)")
                    mm = pe.matmul(ps_v[:, a, :], pair, w_qkv[:, 2 * C:3 * C],
                                   start=True, stop=True)
                mm.then_inc(s_v_ps, 1)

            def scores(i, o):
                g = number(i, o)
                pe.wait_ge(s_qk, g + 1)
                need(pe, s_sub, g)
                for w in range(OCT):
                    a, j = w // 2, w % 2
                    mm = pe.matmul(ps_s[j * GP:(j + 1) * GP, a, 0:NH * N],
                                   keys[:, o % 2, w, :],
                                   queries[:, o % 2, w, :, :].rearrange("p h n -> p (h n)"),
                                   start=True, stop=True)
                mm.then_inc(s_s, 1)

            def attend(i, o):
                g = number(i, o)
                wait_alone(pe, (s_a, g + 1), (s_o, g))
                for a in range(PAIRS):
                    for h in range(NH):
                        for j in range(2):
                            rows = slice(j * GP, j * GP + N)
                            mm = pe.matmul(ps_o[h * HD:(h + 1) * HD, j, a * N:(a + 1) * N],
                                           values[rows, o % VRING, a, h * HD:(h + 1) * HD],
                                           att[rows, o % 2, a, h, :],
                                           start=True, stop=True)
                mm.then_inc(s_o_ps, 1)

            def project(i, o):
                g = number(i, o)
                pe.wait_ge(s_o, g + 1)
                need(pe, s_res, g)
                pe.matmul(ps_p[:, 0:TOK], w_proj[:, :], attended[:, o % 2, :, :], start=True,
                          stop=True).then_inc(s_p, 1)

            def iteration(i, first=False, last=False):
                for o in range(BODY):
                    scores(i, o)
                    if not (last and o == BODY - 1):
                        project_qkv(*ahead(i, o, 1))
                    if not (first and o < 2):
                        project(*ahead(i, o, -2))
                    if not (first and o < 1):
                        attend(*ahead(i, o, -1))

            def image(b, first=False, last=False):
                if first:
                    iteration(b * IPI, first=True)
                with pe.Fori(1 if first else 0, LAST_STATS) as j:
                    iteration(b * IPI + j)
                if not last:
                    group_means(b + 1, number(b * IPI + IPI - 1, -2))
                iteration(b * IPI + IPI - 1, last=last)

            pe.wait_ge(s_w, 48)
            pe.wait_ge(s_pad, 4)
            group_means(0, 0)
            project_qkv(0, 0)
            image(0, first=True)
            with pe.Fori(1, B - 1) as b:
                image(b)
            image(B - 1, last=True)
            project(B * IPI - 1, BODY - 2)
            attend(B * IPI - 1, BODY - 1)
            project(B * IPI - 1, BODY - 1)

        @block.vector
        def _(dve):
            def count(b, j, o, buf):
                if o == 0:
                    dve.wait_ge(s_xs[buf], 16 * (b * (SN // SBUFS) + 1) + (j - buf) * (16 // SBUFS))
                if isinstance(j, int):
                    dst = bn[:, j * BODY + o, :]
                else:
                    dst = bn[:, bass.ds(j * BODY + o, 1), :].rearrange("p a t -> p (a t)")
                ins = dve.bn_stats(dst, x_stat[:, buf, o * BN:(o + 1) * BN])
                if o == BODY - 1:
                    ins.then_inc(s_bn, 1)

            def channel_stats(b):
                wait_alone(dve, (s_bn, b * SN + SN))
                dve.bn_aggr(mv[:, :], bn[:, :, :].rearrange("p a t -> p (a t)")).then_inc(s_mv, 1)

            def group_stats(b):
                done = b * GROUP_STEPS
                dve.wait_ge(s_gm, b + 1)
                dve.wait_ge(s_mv, b + 1)
                dve.tensor_copy(gmean[:, :], ps_p[:, GCOL:GCOL + 1]).then_inc(s_c, 1)
                dve.wait_ge(s_c, done + 1)
                dve.tensor_tensor(dev[:, :], mv[:, 0:1], gmean[:, :], ALU.subtract).then_inc(s_c, 1)
                dve.wait_ge(s_c, done + 2)
                dve.tensor_tensor(dev2[:, :], dev[:, :], dev[:, :], ALU.mult).then_inc(s_c, 1)
                dve.wait_ge(s_c, done + 3)
                dve.tensor_tensor(spread[:, :], mv[:, 1:2], dev2[:, :], ALU.add).then_inc(s_c, 1)
                dve.wait_ge(s_gv, b + 1)
                dve.tensor_scalar(gvar[:, :], ps_p[:, GCOL:GCOL + 1], EPS, None,
                                  ALU.add).then_inc(s_c, 1)

            def subtract_max(i, o):
                g = number(i, o)
                dve.wait_ge(s_s, g + 1)
                dve.tensor_reduce(smax[:, :, :], scores_ps.rearrange("p a h n -> p a n h"), AX.X,
                                  ALU.max).then_inc(s_max, 1)
                dve.wait_ge(s_max, g + 1)
                dve.tensor_tensor(att[:, o % 2, :, :, :], scores_ps,
                                  smax[:, :, :].unsqueeze(2).broadcast_to([P, PAIRS, NH, N]),
                                  ALU.subtract).then_inc(s_sub, 1)

            def normalise_weights(i, o):
                g = number(i, o)
                a = att[:, o % 2, :, :, :]
                dve.wait_ge(s_den, g + 1)
                dve.reciprocal(rden[:, :, :], den[:, o % 2, :, :]).then_inc(s_r, 1)
                dve.wait_ge(s_r, g + 1)
                dve.tensor_tensor(a, a, rden[:, :, :].unsqueeze(2).broadcast_to([P, PAIRS, NH, N]),
                                  ALU.mult).then_inc(s_a, 1)

            def add_residual(i, o):
                slot = o // OPS
                if o % OPS == 0:
                    need(dve, s_st[slot], 16 * i)
                dve.wait_ge(s_p, number(i, o) + 1)
                src = ps_p[:, 0:TOK].rearrange("p (w r c) -> p w r c", w=OCT, c=WS)
                dve.tensor_tensor(octet_pixels(x_out, slot, o % OPS), src,
                                  octet_pixels(x_in, slot, o % OPS), ALU.add).then_inc(s_res, 1)

            def iteration(i, stats=None, first=False):
                for o in range(BODY):
                    if not (first and o < 1):
                        normalise_weights(*ahead(i, o, -1))
                    subtract_max(i, o)
                    if not (first and o < 2):
                        add_residual(*ahead(i, o, -2))
                    if stats:
                        count(*stats[:2], o, stats[2])

            def image(b, first=False, last=False):
                start = 0
                if first:
                    for j in range(SBUFS):
                        iteration(b * IPI + j, (b + 1, j, j), first=j == 0)
                    start = SBUFS
                with dve.Fori(start // SBUFS, SN // SBUFS) as turn:
                    for k in range(SBUFS):
                        j = turn * SBUFS + k
                        iteration(b * IPI + j, None if last else (b + 1, j, k))
                if not last:
                    channel_stats(b + 1)
                for j in range(SN, LAST_STATS):
                    iteration(b * IPI + j)
                if not last:
                    group_stats(b + 1)
                iteration(b * IPI + IPI - 1)

            for j in range(SN):
                for o in range(BODY):
                    count(0, j, o, j % SBUFS)
            channel_stats(0)
            group_stats(0)
            image(0, first=True)
            with dve.Fori(1, B - 1) as b:
                image(b)
            image(B - 1, last=True)
            normalise_weights(B * IPI - 1, BODY - 1)
            add_residual(B * IPI - 1, BODY - 2)
            add_residual(B * IPI - 1, BODY - 1)


def kernel(x, L0_conv_w_qkv, L0_conv_w_proj):
    import numpy as np
    import concourse.bacc as bacc
    from concourse.bass_utils import run_bass_kernel_spmd

    nc = bacc.Bacc("TRN2", target_bir_lowering=False, num_devices=1)
    arrays = {
        "x": np.ascontiguousarray(x),
        "w_qkv_t": np.ascontiguousarray(np.asarray(L0_conv_w_qkv).T),
        "w_proj_t": np.ascontiguousarray(np.asarray(L0_conv_w_proj).T),
        "group_mean": np.kron(np.eye(32, dtype=np.float32), np.full((4, 4), 0.25, np.float32)),
    }
    dt = mybir.dt.float32
    args = [nc.dram_tensor(n, a.shape, dt, kind="ExternalInput").ap() for n, a in arrays.items()]
    out = nc.dram_tensor("out", arrays["x"].shape, dt, kind="ExternalOutput").ap()
    window_attention_groupnorm_kernel(nc, *args, out)
    r = run_bass_kernel_spmd(nc, [arrays], core_ids=[0])
    return r.results[0]["out"]
```

```python
import concourse.bass as bass
from concourse import mybir
from contextlib import ExitStack


def window_attention_groupnorm_kernel(nc, x, w_qkv_t, w_proj_t, group_mean, out):
    FP32 = mybir.dt.float32
    FP32R = mybir.dt.float32r
    ALU = mybir.AluOpType
    ACT = mybir.ActivationFunctionType
    AX = mybir.AxisListType

    B, C, H, W = x.shape
    WS = 7
    N = WS * WS
    NH = 4
    HD = C // NH
    SCALE = HD ** -0.5
    EPS = 1e-5
    GP = 64
    P = 128
    assert C == P and H % WS == 0 and W % WS == 0

    STRIPS = H // WS
    STRIP = WS * W
    OCT = 8
    PAIRS = OCT // 2
    OPS = W // WS // OCT
    TOK = OCT * N
    SLOTS = 4
    BODY = SLOTS * OPS
    IPI = STRIPS // SLOTS
    NOCT = B * STRIPS * OPS
    BANK = 512
    PAIR_COLS = BANK // 2
    RING = 4

    SBUFS = 2
    PARTS = BODY // SBUFS
    BN = 448
    SCH = PARTS * BN
    SN = H * W // SCH
    SITERS = SN // SBUFS
    CLOSE = BODY // 2
    assert SN * SCH == H * W and SITERS == IPI - 1

    x_strip = x.rearrange("b c (s r) w -> b c s (r w)", r=WS)
    out_strip = out.rearrange("b c (s r) w -> b c s (r w)", r=WS)
    x_chunk = x.rearrange("b c h w -> b c (h w)").rearrange("b c (n k) -> b c n k", k=SCH)

    ctx = ExitStack()
    with ctx:
        def sb(name, shape, dtype=FP32):
            return ctx.enter_context(nc.sbuf_tensor(name, shape, dtype))

        def pb(name, shape):
            return ctx.enter_context(nc.psum_tensor(name, shape, FP32))

        def sem(name):
            return ctx.enter_context(nc.semaphore(name))

        w_qkv = sb("w_qkv", [P, 3 * C])
        w_proj = sb("w_proj", [P, C])
        w_high = sb("w_high", [P, 3, C], FP32R)
        w_low = sb("w_low", [P, 3, C], FP32R)
        group = sb("group", [P, P])
        x_stat = sb("x_stat", [P, SBUFS, SCH])
        bn = sb("bn", [P, SN * PARTS, 6])
        mv = sb("mv", [P, 2])
        gmean = sb("gmean", [P, 1])
        dev = sb("dev", [P, 1])
        dev2 = sb("dev2", [P, 1])
        spread = sb("spread", [P, 1])
        gvar = sb("gvar", [P, 1])
        minus_half = sb("minus_half", [P, 1])
        gm_rstd = sb("gm_rstd", [P, 1])
        coef_next = sb("coef_next", [P, 2])
        coef = sb("coef", [P, 2])

        x_in = sb("x_in", [P, SLOTS, STRIP])
        x_out = sb("x_out", [P, SLOTS, STRIP])
        xn = sb("xn", [P, RING, OCT, GP])
        xn_high = sb("xn_high", [P, 2, OCT, N], FP32R)
        xn_low = sb("xn_low", [P, 2, OCT, N], FP32R)
        keys = sb("keys", [P, 2, OCT, GP])
        queries = sb("queries", [P, 2, OCT, NH, N])
        values = sb("values", [P, RING, PAIRS, C])
        att = sb("att", [P, RING, PAIRS, NH, N])
        smax = sb("smax", [P, PAIRS, N])
        half = sb("half", [P, PAIRS, 2, N])
        den = sb("den", [P, 2, PAIRS, N])
        rden = sb("rden", [P, 2, PAIRS, N])
        att_out_high = sb("att_out_high", [P, 2, OCT, N], FP32R)
        att_out_low = sb("att_out_low", [P, 2, OCT, N], FP32R)

        ps_s = pb("ps_scores", [P, PAIRS, PAIR_COLS])
        ps_v = pb("ps_v", [P, PAIRS, C])
        ps_k = pb("ps_k", [P, BANK])
        ps_q = pb("ps_q", [P, BANK])
        ps_o = pb("ps_attended", [P, 2, BANK])
        ps_p = pb("ps_projected", [P, BANK])
        GCOL = BANK - 1
        scores_ps = ps_s[:, :, 0:NH * N].rearrange("p a (h n) -> p a h n", h=NH)

        s_w = sem("weights_loaded")
        s_passed = sem("waits_passed")
        s_pad = sem("pads_zeroed")
        s_xs = [sem(f"stat_chunk_loaded{i}") for i in range(SBUFS)]
        s_bn = sem("bn_done")
        s_mv = sem("channel_stats_ready")
        s_gm = sem("group_mean_in_psum")
        s_c = sem("group_steps_done")
        s_gv = sem("group_var_in_psum")
        s_cp = sem("coef_steps_done")
        s_x = [sem(f"strip_loaded{i}") for i in range(SLOTS)]
        s_st = [sem(f"strip_stored{i}") for i in range(SLOTS)]
        s_wh = sem("weights_high_ready")
        s_wl = sem("weights_low_ready")
        s_xn = sem("normalised")
        s_xh = sem("tokens_high_ready")
        s_xl = sem("tokens_low_ready")
        s_q_ps = sem("q_in_psum")
        s_k_ps = sem("k_in_psum")
        s_v_ps = sem("v_in_psum")
        s_qk = sem("qk_copied")
        s_v = sem("v_copied")
        s_s = sem("scores_ready")
        s_max = sem("max_ready")
        s_sub = sem("max_subtracted")
        s_e = sem("exp_ready")
        s_half = sem("half_sums_ready")
        s_den = sem("denominator_ready")
        s_r = sem("reciprocal_ready")
        s_a = sem("weights_normalised")
        s_o_ps = sem("attended_in_psum")
        s_oh = sem("attended_high_copied")
        s_ol = sem("attended_low_copied")
        s_p = sem("projected")
        s_res = sem("residual_added")

        GROUP_STEPS = 5
        COEF_STEPS = 4

        def need(eng, semaphore, value):
            if not isinstance(value, int) or value > 0:
                eng.wait_ge(semaphore, value)

        def wait_alone(eng, *waits):
            for semaphore, value in waits:
                need(eng, semaphore, value)
            eng.sem_inc(s_passed, 1)

        def octet_pixels(buffer, slot, o):
            part = buffer[:, slot, :].rearrange("p (r w c) -> p w r c", r=WS, c=WS)
            return part[:, o * OCT:(o + 1) * OCT, :, :]

        def ahead(i, o, by):
            return i + (o + by) // BODY, (o + by) % BODY

        def number(i, o):
            return i * BODY + o

        def plain(ap):
            return ap.bitcast(FP32)

        def by_parity(buffer):
            return buffer.rearrange("p (a j) n -> p j a n", j=2)

        attended_ps = ps_o[:, :, 0:PAIRS * N].rearrange("p j (a n) -> p j a n", n=N)

        block = ctx.enter_context(nc.Block())

        @block.sync
        def _(sp):
            def one(view, b, s):
                if isinstance(b, int) and isinstance(s, int):
                    return view[b, :, s, :]
                pick = lambda v: slice(v, v + 1) if isinstance(v, int) else bass.ds(v, 1)
                return view[pick(b), :, pick(s), :].rearrange("a c s w -> (a c s) w")

            def load(b, s, slot):
                sp.dma_start(x_in[:, slot, :], one(x_strip, b, s)).then_inc(s_x[slot], 16)

            def stat_load(b, n, buf):
                need(sp, s_bn, (b * SN + n - SBUFS + 1))
                sp.dma_start(x_stat[:, buf, :], one(x_chunk, b, n)).then_inc(s_xs[buf], 16)

            def iteration(b, j, next_strips, chunks=None):
                for slot in range(SLOTS):
                    sp.wait_ge(s_res, number(b * IPI + j, (slot + 1) * OPS))
                    sp.dma_start(one(out_strip, b, j * SLOTS + slot),
                                 x_out[:, slot, :]).then_inc(s_st[slot], 16)
                    if next_strips:
                        load(next_strips[0], next_strips[1] + slot, slot)
                    if chunks and slot >= SLOTS - SBUFS:
                        k = slot - (SLOTS - SBUFS)
                        stat_load(chunks[0], chunks[1] + k, k)

            def image(b, behind_next=True, last=False):
                with sp.Fori(0, SITERS - 1) as j:
                    iteration(b, j, (b, j * SLOTS + SLOTS),
                              None if last else (b + 1, j * SBUFS + SBUFS))
                iteration(b, SITERS - 1, (b, SITERS * SLOTS))
                if behind_next:
                    for n in range(SBUFS):
                        stat_load(b + 2, n, n)
                iteration(b, IPI - 1, None if last else (b + 1, 0))

            sp.dma_start(w_qkv[:, :], w_qkv_t).then_inc(s_w, 16)
            sp.dma_start(w_proj[:, :], w_proj_t).then_inc(s_w, 16)
            sp.dma_start(group[:, :], group_mean).then_inc(s_w, 16)
            for n in range(SN):
                stat_load(0, n, n % SBUFS)
            for slot in range(SLOTS):
                load(0, slot, slot)
            for n in range(SBUFS):
                stat_load(1, n, n)
            image(0)
            with sp.Fori(1, B - 2) as b:
                image(b)
            image(B - 2, behind_next=False)
            image(B - 1, behind_next=False, last=True)
            for slot in range(SLOTS):
                sp.wait_ge(s_st[slot], 16 * B * IPI)

        @block.gpsimd
        def _(pool):
            pool.memset(xn[:, :, :, :], 0.0).then_inc(s_pad, 1)
            pool.memset(keys[:, :, :, :], 0.0).then_inc(s_pad, 1)
            pool.memset(queries[:, :, :, :, :], 0.0).then_inc(s_pad, 1)
            pool.memset(minus_half[:, :], -0.5).then_inc(s_pad, 1)
            pool.wait_ge(s_pad, 4)

            def coefficients(b):
                done = b * (COEF_STEPS + 1)
                pool.wait_ge(s_c, b * GROUP_STEPS + GROUP_STEPS)
                pool.tensor_tensor(coef_next[:, 0:1], gvar[:, :], minus_half[:, :],
                                   ALU.pow).then_inc(s_cp, 1)
                pool.wait_ge(s_cp, done + 1)
                pool.tensor_tensor(gm_rstd[:, :], gmean[:, :], coef_next[:, 0:1],
                                   ALU.mult).then_inc(s_cp, 1)
                wait_alone(pool, (s_cp, done + 2))
                pool.tensor_scalar(coef_next[:, 1:2], gm_rstd[:, :], -1.0, 0.0, ALU.mult,
                                   ALU.add).then_inc(s_cp, 2)

            def choose(b):
                wait_alone(pool, (s_cp, b * (COEF_STEPS + 1) + COEF_STEPS))
                pool.tensor_copy(coef[:, :], coef_next[:, :]).then_inc(s_cp, 1)
                wait_alone(pool, (s_cp, b * (COEF_STEPS + 1) + COEF_STEPS + 1))

            def normalise(i, o):
                g = number(i, o)
                wait_alone(pool, (s_x[o // OPS], 16 * i + 16), (s_v_ps, g - RING + 1))
                dst = xn[:, o % RING, :, 0:N].rearrange("p w (r c) -> p w r c", r=WS)
                pool.tensor_scalar(dst, octet_pixels(x_in, o // OPS, o % OPS), coef[:, 0:1],
                                   coef[:, 1:2], ALU.mult, ALU.add).then_inc(s_xn, 1)

            def low_part(i, o):
                pool.wait_ge(s_xh, number(i, o) + 1)
                pool.tensor_tensor(xn_low[:, o % 2, :, :], xn[:, o % RING, :, 0:N],
                                   plain(xn_high[:, o % 2, :, :]), ALU.subtract).then_inc(s_xl, 1)

            def sum_heads(i, o):
                g = number(i, o)
                a = att[:, o % RING, :, :, :]
                pool.wait_ge(s_e, g + 1)
                need(pool, s_den, g)
                pool.tensor_tensor(half[:, :, :, :], a[:, :, 0:2, :], a[:, :, 2:4, :],
                                   ALU.add).then_inc(s_half, 1)
                pool.wait_ge(s_half, g + 1)
                pool.tensor_tensor(den[:, o % 2, :, :], half[:, :, 0, :], half[:, :, 1, :],
                                   ALU.add).then_inc(s_den, 1)

            def normalise_weights(i, o):
                a = att[:, o % RING, :, :, :]
                pool.wait_ge(s_r, number(i, o) + 1)
                pool.tensor_tensor(a, a, rden[:, o % 2, :, :].unsqueeze(2).broadcast_to(
                    [P, PAIRS, NH, N]), ALU.mult).then_inc(s_a, 1)

            def iteration(i, next_image=None, first=False, last=False):
                for o in range(BODY):
                    if next_image is not None and o == CLOSE:
                        coefficients(next_image)
                    ni, no = ahead(i, o, 3)
                    if no == 0 and next_image is not None:
                        choose(next_image)
                    if not (last and o + 3 >= BODY):
                        normalise(ni, no)
                    if not (last and o + 2 >= BODY):
                        low_part(*ahead(i, o, 2))
                    sum_heads(i, o)
                    if not (first and o < 1):
                        normalise_weights(*ahead(i, o, -1))

            coefficients(0)
            choose(0)
            for o in range(3):
                normalise(0, o)
            for o in range(2):
                low_part(0, o)

            def image(b, first=False, last=False):
                if first:
                    iteration(b * IPI, first=True)
                with pool.Fori(1 if first else 0, IPI - 1) as j:
                    iteration(b * IPI + j)
                iteration(b * IPI + IPI - 1, next_image=None if last else b + 1, last=last)

            image(0, first=True)
            with pool.Fori(1, B - 1) as b:
                image(b)
            image(B - 1, last=True)
            normalise_weights(B * IPI - 1, BODY - 1)

        @block.scalar
        def _(act):
            def copy_qk(i, o):
                g = number(i, o)
                act.wait_ge(s_q_ps, g + 1)
                for h in range(NH):
                    rows = slice(h * HD, (h + 1) * HD)
                    act.activation(queries[rows, o % 2, :, h, :],
                                   ps_q[rows, 0:TOK].rearrange("p (w n) -> p w n", n=N), ACT.Copy)
                act.wait_ge(s_k_ps, g + 1)
                act.activation(keys[:, o % 2, :, 0:N],
                               ps_k[:, 0:TOK].rearrange("p (w n) -> p w n", n=N),
                               ACT.Copy).then_inc(s_qk, 1)

            def high_part(i, o):
                g = number(i, o)
                act.wait_ge(s_xn, g + 1)
                need(act, s_k_ps, g - 1)
                act.activation(xn_high[:, o % 2, :, :], xn[:, o % RING, :, 0:N],
                               ACT.Copy).then_inc(s_xh, 1)

            def copy_v(i, o):
                act.wait_ge(s_v_ps, number(i, o) + 1)
                act.activation(values[:, o % RING, :, :], ps_v[:, :, :], ACT.Copy).then_inc(s_v, 1)

            def exp(i, o):
                a = att[:, o % RING, :, :, :]
                act.wait_ge(s_sub, number(i, o) + 1)
                act.activation(a, a, ACT.Exp, scale=SCALE).then_inc(s_e, 1)

            def copy_attended(i, o):
                act.wait_ge(s_o_ps, number(i, o) + 1)
                act.activation(by_parity(att_out_high[:, o % 2, :, :]), attended_ps,
                               ACT.Copy).then_inc(s_oh, 1)

            def iteration(i, first=False, last=False):
                for o in range(BODY):
                    if not (last and o >= BODY - 2):
                        high_part(*ahead(i, o, 2))
                    if not (last and o == BODY - 1):
                        copy_qk(*ahead(i, o, 1))
                    exp(i, o)
                    if not (last and o == BODY - 1):
                        copy_v(*ahead(i, o, 1))
                    if not (first and o < 2):
                        copy_attended(*ahead(i, o, -2))

            act.wait_ge(s_w, 48)
            act.activation(w_high[:, 0:2, :].rearrange("p a c -> p (a c)"), w_qkv[:, 0:2 * C],
                           ACT.Copy).then_inc(s_wh, 1)
            act.activation(w_high[:, 2, :], w_proj[:, :], ACT.Copy).then_inc(s_wh, 1)
            act.wait_ge(s_pad, 4)
            high_part(0, 0)
            high_part(0, 1)
            copy_qk(0, 0)
            copy_v(0, 0)
            iteration(0, first=True)
            with act.Fori(1, B * IPI - 1) as i:
                iteration(i)
            iteration(B * IPI - 1, last=True)
            copy_attended(B * IPI - 1, BODY - 2)
            copy_attended(B * IPI - 1, BODY - 1)

        @block.tensor
        def _(pe):
            def group_means(b, projected):
                wait_alone(pe, (s_mv, b + 1), (s_res, projected))
                pe.matmul(ps_p[:, GCOL:GCOL + 1], group[:, :], mv[:, 0:1], start=True,
                          stop=True).then_inc(s_gm, 1)
                pe.wait_ge(s_c, b * GROUP_STEPS + GROUP_STEPS - 1)
                pe.matmul(ps_p[:, GCOL:GCOL + 1], group[:, :], spread[:, :], start=True,
                          stop=True).then_inc(s_gv, 1)
                wait_alone(pe, (s_c, b * GROUP_STEPS + GROUP_STEPS))

            def three_passes(out_ps, w, high, low):
                pe.matmul(out_ps, w_high[:, w, :], high, start=True, stop=False)
                pe.matmul(out_ps, w_high[:, w, :], low, start=False, stop=False)
                return pe.matmul(out_ps, w_low[:, w, :], high, start=False, stop=True)

            def project_qkv(i, o):
                g = number(i, o)
                high, low = xn_high[:, o % 2, :, :], xn_low[:, o % 2, :, :]
                pe.wait_ge(s_xl, g + 1)
                need(pe, s_qk, g)
                three_passes(ps_q[:, 0:TOK], 0, high, low).then_inc(s_q_ps, 1)
                three_passes(ps_k[:, 0:TOK], 1, high, low).then_inc(s_k_ps, 1)
                need(pe, s_v, g)
                for a in range(PAIRS):
                    pair = xn[:, o % RING, 2 * a:2 * a + 2, :].rearrange("p j n -> p (j n)")
                    mm = pe.matmul(ps_v[:, a, :], pair, w_qkv[:, 2 * C:3 * C],
                                   start=True, stop=True)
                mm.then_inc(s_v_ps, 1)

            def scores(i, o):
                g = number(i, o)
                pe.wait_ge(s_qk, g + 1)
                need(pe, s_sub, g)
                for w in range(OCT):
                    a, j = w // 2, w % 2
                    mm = pe.matmul(ps_s[j * GP:(j + 1) * GP, a, 0:NH * N],
                                   keys[:, o % 2, w, :],
                                   queries[:, o % 2, w, :, :].rearrange("p h n -> p (h n)"),
                                   start=True, stop=True)
                mm.then_inc(s_s, 1)

            def attend(i, o):
                g = number(i, o)
                wait_alone(pe, (s_a, g + 1), (s_ol, g))
                for a in range(PAIRS):
                    for h in range(NH):
                        for j in range(2):
                            rows = slice(j * GP, j * GP + N)
                            mm = pe.matmul(ps_o[h * HD:(h + 1) * HD, j, a * N:(a + 1) * N],
                                           values[rows, o % RING, a, h * HD:(h + 1) * HD],
                                           att[rows, o % RING, a, h, :],
                                           start=True, stop=True)
                mm.then_inc(s_o_ps, 1)

            def project(i, o):
                g = number(i, o)
                pe.wait_ge(s_ol, g + 1)
                need(pe, s_res, g)
                three_passes(ps_p[:, 0:TOK], 2, att_out_high[:, o % 2, :, :],
                             att_out_low[:, o % 2, :, :]).then_inc(s_p, 1)

            def iteration(i, first=False, last=False, next_image=None):
                for o in range(BODY):
                    if next_image is not None and o == CLOSE:
                        group_means(next_image, number(i, o - 3))
                    scores(i, o)
                    if not (last and o == BODY - 1):
                        project_qkv(*ahead(i, o, 1))
                    if not (first and o < 3):
                        project(*ahead(i, o, -3))
                    if not (first and o < 2):
                        attend(*ahead(i, o, -2))

            def image(b, first=False, last=False):
                if first:
                    iteration(b * IPI, first=True)
                with pe.Fori(1 if first else 0, IPI - 1) as j:
                    iteration(b * IPI + j)
                iteration(b * IPI + IPI - 1, last=last, next_image=None if last else b + 1)

            pe.wait_ge(s_w, 48)
            pe.wait_ge(s_pad, 4)
            group_means(0, 0)
            pe.wait_ge(s_wl, 2)
            project_qkv(0, 0)
            image(0, first=True)
            with pe.Fori(1, B - 1) as b:
                image(b)
            image(B - 1, last=True)
            end = B * IPI - 1
            project(end, BODY - 3)
            attend(end, BODY - 2)
            project(end, BODY - 2)
            attend(end, BODY - 1)
            project(end, BODY - 1)

        @block.vector
        def _(dve):
            def count(b, j, k, o):
                if o == 0:
                    dve.wait_ge(s_xs[k], 16 * (b * SITERS + j) + 16)
                part = (j * SBUFS + k) * PARTS + o
                if isinstance(part, int):
                    dst = bn[:, part, :]
                else:
                    dst = bn[:, bass.ds(part, 1), :].rearrange("p a t -> p (a t)")
                ins = dve.bn_stats(dst, x_stat[:, k, o * BN:(o + 1) * BN])
                if o == PARTS - 1:
                    ins.then_inc(s_bn, 1)

            def channel_stats(b):
                wait_alone(dve, (s_bn, b * SN + SN))
                dve.bn_aggr(mv[:, :], bn[:, :, :].rearrange("p a t -> p (a t)")).then_inc(s_mv, 1)

            def group_stats(b):
                done = b * GROUP_STEPS
                dve.wait_ge(s_gm, b + 1)
                dve.wait_ge(s_mv, b + 1)
                dve.tensor_copy(gmean[:, :], ps_p[:, GCOL:GCOL + 1]).then_inc(s_c, 1)
                dve.wait_ge(s_c, done + 1)
                dve.tensor_tensor(dev[:, :], mv[:, 0:1], gmean[:, :], ALU.subtract).then_inc(s_c, 1)
                dve.wait_ge(s_c, done + 2)
                dve.tensor_tensor(dev2[:, :], dev[:, :], dev[:, :], ALU.mult).then_inc(s_c, 1)
                dve.wait_ge(s_c, done + 3)
                dve.tensor_tensor(spread[:, :], mv[:, 1:2], dev2[:, :], ALU.add).then_inc(s_c, 1)
                dve.wait_ge(s_gv, b + 1)
                dve.tensor_scalar(gvar[:, :], ps_p[:, GCOL:GCOL + 1], EPS, None,
                                  ALU.add).then_inc(s_c, 1)

            def subtract_max(i, o):
                g = number(i, o)
                dve.wait_ge(s_s, g + 1)
                dve.tensor_reduce(smax[:, :, :], scores_ps.rearrange("p a h n -> p a n h"), AX.X,
                                  ALU.max).then_inc(s_max, 1)
                dve.wait_ge(s_max, g + 1)
                dve.tensor_tensor(att[:, o % RING, :, :, :], scores_ps,
                                  smax[:, :, :].unsqueeze(2).broadcast_to([P, PAIRS, NH, N]),
                                  ALU.subtract).then_inc(s_sub, 1)

            def reciprocal(i, o):
                g = number(i, o)
                dve.wait_ge(s_den, g + 1)
                need(dve, s_a, g - 1)
                dve.reciprocal(rden[:, o % 2, :, :], den[:, o % 2, :, :]).then_inc(s_r, 1)

            def attended_low(i, o):
                dve.wait_ge(s_oh, number(i, o) + 1)
                dve.tensor_tensor(by_parity(att_out_low[:, o % 2, :, :]), attended_ps,
                                  by_parity(plain(att_out_high[:, o % 2, :, :])),
                                  ALU.subtract).then_inc(s_ol, 1)

            def add_residual(i, o):
                slot = o // OPS
                if o % OPS == 0:
                    need(dve, s_st[slot], 16 * i)
                dve.wait_ge(s_p, number(i, o) + 1)
                src = ps_p[:, 0:TOK].rearrange("p (w r c) -> p w r c", w=OCT, c=WS)
                dve.tensor_tensor(octet_pixels(x_out, slot, o % OPS), src,
                                  octet_pixels(x_in, slot, o % OPS), ALU.add).then_inc(s_res, 1)

            def iteration(i, stats=None, first=False, next_image=None):
                for o in range(BODY):
                    if next_image is not None and o == CLOSE:
                        group_stats(next_image)
                    if not (first and o < 3):
                        attended_low(*ahead(i, o, -3))
                    subtract_max(i, o)
                    if not (first and o < 1):
                        reciprocal(*ahead(i, o, -1))
                    if not (first and o < 3):
                        add_residual(*ahead(i, o, -3))
                    if stats:
                        count(*stats, o // PARTS, o % PARTS)

            def image(b, first=False, last=False):
                if first:
                    iteration(b * IPI, (b + 1, 0), first=True)
                with dve.Fori(1 if first else 0, SITERS) as j:
                    iteration(b * IPI + j, None if last else (b + 1, j))
                if not last:
                    channel_stats(b + 1)
                iteration(b * IPI + IPI - 1, next_image=None if last else b + 1)

            dve.wait_ge(s_wh, 2)
            dve.tensor_tensor(w_low[:, 0:2, :].rearrange("p a c -> p (a c)"), w_qkv[:, 0:2 * C],
                              plain(w_high[:, 0:2, :]).rearrange("p a c -> p (a c)"),
                              ALU.subtract).then_inc(s_wl, 1)
            dve.tensor_tensor(w_low[:, 2, :], w_proj[:, :], plain(w_high[:, 2, :]),
                              ALU.subtract).then_inc(s_wl, 1)
            for j in range(SITERS):
                for o in range(BODY):
                    count(0, j, o // PARTS, o % PARTS)
            channel_stats(0)
            group_stats(0)
            image(0, first=True)
            with dve.Fori(1, B - 1) as b:
                image(b)
            image(B - 1, last=True)
            end = B * IPI - 1
            reciprocal(end, BODY - 1)
            for o in range(BODY - 3, BODY):
                attended_low(end, o)
                add_residual(end, o)


def kernel(x, L0_conv_w_qkv, L0_conv_w_proj):
    import numpy as np
    import concourse.bacc as bacc
    from concourse.bass_utils import run_bass_kernel_spmd

    nc = bacc.Bacc("TRN2", target_bir_lowering=False, num_devices=1)
    arrays = {
        "x": np.ascontiguousarray(x),
        "w_qkv_t": np.ascontiguousarray(np.asarray(L0_conv_w_qkv).T),
        "w_proj_t": np.ascontiguousarray(np.asarray(L0_conv_w_proj).T),
        "group_mean": np.kron(np.eye(32, dtype=np.float32), np.full((4, 4), 0.25, np.float32)),
    }
    dt = mybir.dt.float32
    args = [nc.dram_tensor(n, a.shape, dt, kind="ExternalInput").ap() for n, a in arrays.items()]
    out = nc.dram_tensor("out", arrays["x"].shape, dt, kind="ExternalOutput").ap()
    window_attention_groupnorm_kernel(nc, *args, out)
    r = run_bass_kernel_spmd(nc, [arrays], core_ids=[0])
    return r.results[0]["out"]
```
